# Optimizing a Trainium2 kernel written in Bass

```python
import numpy as np
import jax
import jax.numpy as jnp

def _softmax(x, axis=-1):
    return jax.nn.softmax(x, axis=axis)

def _gelu(x):
    return jax.nn.gelu(x, approximate=True)

def _silu(x):
    return jax.nn.silu(x)

def _sigmoid(x):
    return jax.nn.sigmoid(x)

def _layernorm(x, axis=-1, eps=1e-05):
    m = jnp.mean(x, axis=axis, keepdims=True)
    v = jnp.var(x, axis=axis, keepdims=True)
    return (x - m) / jnp.sqrt(v + eps)

def _scatter_add(tgt, idx, src, axis=0):
    return tgt.at[idx].add(src)

def _segment_sum(src, seg, n):
    return jax.ops.segment_sum(src, seg, n)
kernel_name = 'mk_cond_resid_d1_seqx_r2_e607f8'

def setup_inputs(seed: int=0):
    np.random.seed(seed)
    _w = jnp.asarray

    def _rec_inputs():
        import jax
        import jax.numpy as jnp
        _rk = jax.random.key(seed)
        x = -0.000125 + 0.9999 * jax.random.normal(jax.random.fold_in(_rk, 1), (32, 128, 512), jnp.float32)
        _lenS = 128 - jax.random.randint(jax.random.fold_in(_rk, 7), (32,), 0, max(1, 128 // 4) + 1, jnp.int32)
        _lenS2 = 128 - jax.random.randint(jax.random.fold_in(_rk, 8), (32,), 0, max(1, 128 // 4) + 1, jnp.int32)
        cond_1024 = -0.00493535 + 1.00056 * jax.random.normal(jax.random.fold_in(_rk, 11), (32, 512), jnp.float32)
        return (x, cond_1024)
    x, cond_1024 = _rec_inputs()

    def _L0_cond_setup():
        import jax, jax.numpy as jnp
        import numpy as np
        import math
        N, T, D, H = (64, 256, 512, 512)
        key = jax.random.key(seed)
        k1, k2, k3, k4 = jax.random.split(key, 4)
        x = jax.random.normal(k1, (N, T, D), dtype=jnp.float32)
        h0 = jax.random.normal(k2, (N, H), dtype=jnp.float32)
        Wx = jax.random.normal(k3, (D, 4 * H), dtype=jnp.float32) / math.sqrt(D)
        Wh = jax.random.normal(k4, (H, 4 * H), dtype=jnp.float32) / math.sqrt(H)
        b = jnp.zeros((4 * H,), dtype=jnp.float32)
        return {'x': x, 'h0': h0, 'Wx': Wx, 'Wh': Wh, 'b': b}
    _L0_cond_all = _L0_cond_setup()
    _L0_cond_in = {k: v for k, v in _L0_cond_all.items() if k in ('Wx', 'Wh', 'b')}
    del _L0_cond_all
    return {'x': x, 'cond_1024': cond_1024, 'L0_cond_Wx': _L0_cond_in['Wx'], 'L0_cond_Wh': _L0_cond_in['Wh'], 'L0_cond_b': _L0_cond_in['b']}

def reference(x, cond_1024, L0_cond_Wx, L0_cond_Wh, L0_cond_b):
    import jax
    import jax.numpy as jnp

    def _L0_cond_ref(x, h0, Wx, Wh, b):
        import jax, jax.numpy as jnp
        import numpy as np
        import math
        N, T, D, H = (64, 256, 512, 512)
        Hdim = h0.shape[1]
        xW = jnp.einsum('ntd,dg->ntg', x, Wx) + b

        def step(carry, xw_t):
            prev_h, prev_c = carry
            a = xw_t + prev_h @ Wh
            i = jax.nn.sigmoid(a[:, :Hdim])
            f = jax.nn.sigmoid(a[:, Hdim:2 * Hdim])
            o = jax.nn.sigmoid(a[:, 2 * Hdim:3 * Hdim])
            g = jnp.tanh(a[:, 3 * Hdim:])
            next_c = f * prev_c + i * g
            next_h = o * jnp.tanh(next_c)
            return ((next_h, next_c), next_h)
        c0 = jnp.zeros_like(h0)
        _, hs = jax.lax.scan(step, (h0, c0), jnp.swapaxes(xW, 0, 1))
        return jnp.swapaxes(hs, 0, 1)
    x = x + _L0_cond_ref(x, cond_1024, L0_cond_Wx, L0_cond_Wh, L0_cond_b)
    return x

_drawn_inputs = setup_inputs


def setup_inputs(seed=0):
    import zlib

    import numpy as np

    out = dict(_drawn_inputs(seed))
    spreads = {'L0_cond_b': (0.0, 0.1)}
    factors = {'cond_1024': 3.314}
    for name, (base, spread) in spreads.items():
        noise = np.random.default_rng([zlib.crc32(name.encode()), seed]).standard_normal(out[name].shape)
        drawn = base * np.exp(spread * noise) if base else spread * noise
        out[name] = jnp.asarray(drawn.astype(out[name].dtype))
    for name, factor in factors.items():
        out[name] = (out[name] * factor).astype(out[name].dtype)
    return out
```

```python
import concourse.bass as bass
from concourse import mybir
from contextlib import ExitStack


F32 = mybir.dt.float32
F16 = mybir.dt.float16
I32 = mybir.dt.int32
ALU = mybir.AluOpType
ACT = mybir.ActivationFunctionType
AX = mybir.AxisListType.X

P = 128
Q = 32
TB = 4
RING = 8
BANKS = 4
AHEAD_PRODUCT = 2
AHEAD_SPLIT = 3
AHEAD_LOAD = 4
HEAD = 14
H_SCALE = float(2 ** HEAD)
TINY = 2.0 ** -60
ONE_EXP = 1 << 23
HI, LO = 0, 1
OUT_FREE = 16
H_FREE = 2
PRODUCTS = ((HI, HI), (HI, LO), (LO, HI))


def lstm_kernel(nc: bass.Bass, x: bass.AP, h0: bass.AP, wx: bass.AP, wh: bass.AP, bias: bass.AP,
                out: bass.AP):
    B, T, D = x.shape
    H = h0.shape[1]
    G = wx.shape[1] // H
    K = D // P
    J = H // P
    M = P // Q
    GC = G * P
    NBLK = T // TB
    LOOPS = (NBLK - AHEAD_LOAD) // 2
    assert B == Q and D == H and J * B == P and TB * B == P and G == 4 and GC == 512

    x_rows = x.rearrange("b (q t) d -> q t b d", t=TB)
    x_units = x.rearrange("b (q t) (j c) -> q j b t c", t=TB, j=J)
    out_units = out.rearrange("b (q t) (j c) -> q j b t c", t=TB, j=J)
    wx_rows = wx.rearrange("(k p) n -> k p n", p=P)
    wh_rows = wh.rearrange("(j m x) n -> m j x n", m=M, x=Q)

    ctx = ExitStack()
    with ctx:
        def sb(name, shape, dt):
            return ctx.enter_context(nc.sbuf_tensor(name, shape, dt))

        def pb(name, shape, dt):
            return ctx.enter_context(nc.psum_tensor(name, shape, dt))

        def sem(name):
            return ctx.enter_context(nc.semaphore(name))

        wx_raw = sb("wx_raw", [P, K, G * H], F32)
        wh_raw = sb("wh_raw", [P, M, G * H], F32)
        wx_part = sb("wx_part", [P, 2, K, J, GC], F16)
        wh_part = sb("wh_part", [P, 2, M, J, GC], F16)
        bias_all = sb("bias_all", [P, G * H], F32)
        w_max = sb("w_max", [P, 2, K], F32)
        w_max1 = sb("w_max1", [P, 2], F32)
        w_top = sb("w_top", [P, 2], F32)
        w_exp = sb("w_exp", [P, 2], I32)
        w_scale = sb("w_scale", [P, 2], I32)
        w_unscale = sb("w_unscale", [P, 2], I32)
        seed_scale = sb("seed_scale", [P, 1], F32)
        gate_unscale = sb("gate_unscale", [P, 1], I32)
        ident = sb("ident", [P, P], F16)
        zeros = sb("zeros", [P, GC], F16)

        x_in = sb("x_in", [P, 2, D], F32)
        x_max = sb("x_max", [P, 1], F32)
        x_exp = sb("x_exp", [P, 1], I32)
        x_scale = sb("x_scale", [P, 1], I32)
        x_unscale = sb("x_unscale", [P, 1], I32)
        xw_scale = sb("xw_scale", [P, 2], F32)
        x_part = sb("x_part", [P, 2, 2, D], F16)
        xT = sb("xT", [P, 2, 2, K, P], F16)
        xw = sb("xw", [P, J, GC], F32)
        seeds = sb("seeds", [P, 2, TB, GC], F32)

        h0_in = sb("h0_in", [B, H], F32)
        h0_max = sb("h0_max", [B, 1], F32)
        h0_exp = sb("h0_exp", [B, 1], I32)
        h0_scale = sb("h0_scale", [B, 1], I32)
        h0_unscale = sb("h0_unscale", [B, 1], I32)
        h0_rel = sb("h0_rel", [B, 1], F32)
        h0_part = sb("h0_part", [B, 2, H], F16)
        h0_units = sb("h0_units", [P, 2, P], F16)
        h0_rel_all = sb("h0_rel_all", [P, 1], F32)
        h0_prod = sb("h0_prod", [P, GC], F32)
        seed0 = sb("seed0", [P, GC], F32)

        if_act = sb("if_act", [P, 2, 2, P], F32)
        g_act = sb("g_act", [P, 2, P], F32)
        o_act = sb("o_act", [P, 2, P], F32)
        fc = sb("fc", [P, P], F32)
        ig = sb("ig", [P, P], F32)
        c = sb("c", [P, 2, P], F32)
        tc = sb("tc", [P, 2, P], F32)
        h = sb("h", [P, 2, P], F32)
        h_part = sb("h_part", [P, 2, P], F16)
        hT = sb("hT", [P, 2, 2, M, B], F16)
        x_res = sb("x_res", [P, 2, TB, P], F32)
        out_buf = sb("out_buf", [P, 2, TB, P], F32)

        gates = [pb(f"gates{n}", [P, GC], F32) for n in range(BANKS)]
        xp = [pb(f"xp{n}", [P, GC], F32) for n in range(2)]
        trp = pb("trp", [P, 2, K, P], F16)

        wx_in = [sem(f"wx_in{k}") for k in range(K)]
        wh_in = [sem(f"wh_in{k}") for k in range(M)]
        bias_in = sem("bias_in")
        h0_loaded = sem("h0_loaded")
        h0_moved = sem("h0_moved")
        x_in_loaded = [sem(f"x_in_loaded{n}") for n in range(2)]
        x_res_loaded = [sem(f"x_res_loaded{n}") for n in range(2)]
        seeds_moved = [sem(f"seeds_moved{n}") for n in range(2)]
        out_stored = [sem(f"out_stored{n}") for n in range(2)]
        const_ready = sem("const_ready")
        w_max_ready = sem("w_max_ready")
        w_top_ready = sem("w_top_ready")
        w_scale_ready = sem("w_scale_ready")
        w_hi_ready = sem("w_hi_ready")
        wx_ready = sem("wx_ready")
        wh_ready = sem("wh_ready")
        small = sem("small")
        banks_open = sem("banks_open")
        h0_parts_ready = sem("h0_parts_ready")
        h0_product = sem("h0_product")
        x_max_ready = sem("x_max_ready")
        x_hi_ready = sem("x_hi_ready")
        x_part_ready = sem("x_part_ready")
        x_turned = sem("x_turned")
        xT_ready = sem("xT_ready")
        xp_done = sem("xp_done")
        xw_ready = sem("xw_ready")
        seeded = sem("seeded")
        gates_done = sem("gates_done")
        if_ready = sem("if_ready")
        g_ready = sem("g_ready")
        o_ready = sem("o_ready")
        fc_ready = sem("fc_ready")
        ig_ready = sem("ig_ready")
        c_ready = sem("c_ready")
        tc_ready = sem("tc_ready")
        h_hi_ready = sem("h_hi_ready")
        hT_hi_ready = sem("hT_hi_ready")
        h_ready = sem("h_ready")
        h_lo_ready = sem("h_lo_ready")
        hT_lo_ready = sem("hT_lo_ready")
        out_ready = sem("out_ready")

        f32v = lambda t: t.bitcast(F32)
        has = lambda i, n: not isinstance(i, int) or 0 <= 2 * i + n < NBLK
        block_of = lambda i, n: 2 * i + n
        uses = lambda i, n: i + n // 2 + 1

        block = ctx.enter_context(nc.Block())

        @block.sync
        def _(sp):
            def load_x(i, n):
                if has(i, n):
                    if has(i, n - 2):
                        sp.wait_ge(x_part_ready, block_of(i, n - 2) + 1)
                    for t in range(TB):
                        sp.dma_start(x_in[Q * t:Q * t + Q, n % 2, :],
                                     x_rows[block_of(i, n), t, :, :]).then_inc(x_in_loaded[n % 2], 16)

            def load_residual(i, n):
                if has(i, n):
                    for j in range(J):
                        sp.dma_start(x_res[Q * j:Q * j + Q, n % 2, :, :],
                                     x_units[block_of(i, n), j, :, :, :]).then_inc(x_res_loaded[n % 2], 16)

            def move_seeds(i, n, j):
                if has(i, n):
                    sp.wait_ge(xw_ready, TB * block_of(i, n) + j + 1)
                    for t in range(TB):
                        sp.dma_start(seeds[Q * j:Q * j + Q, n % 2, t, :],
                                     xw[Q * t:Q * t + Q, j, :]).then_inc(seeds_moved[n % 2], 16)

            def block_dmas(i, n):
                load_x(i, n + AHEAD_LOAD)
                for j in range(J):
                    if j == 0 and has(i, n + AHEAD_PRODUCT):
                        sp.wait_ge(seeded, TB * block_of(i, n) + TB - 1)
                    move_seeds(i, n + AHEAD_PRODUCT, j)
                sp.wait_ge(out_ready, H_FREE + TB * block_of(i, n) + TB)
                for j in range(J):
                    sp.dma_start(out_units[block_of(i, n), j, :, :, :],
                                 out_buf[Q * j:Q * j + Q, n % 2, :, :]).then_inc(out_stored[n % 2], 16)
                load_residual(i, n + 2)

            for n in range(2):
                sp.sem_inc(out_stored[n], OUT_FREE)
            load_x(0, 0)
            sp.dma_start(h0_in[:, :], h0).then_inc(h0_loaded, 16)
            for k in range(K):
                sp.dma_start(wx_raw[:, k, :], wx_rows[k, :, :]).then_inc(wx_in[k], 16)
            load_x(0, 1)
            sp.dma_start(bias_all[:, :], bias.rearrange("(a n) -> a n", a=1).broadcast_to([P, G * H]))\
              .then_inc(bias_in, 16)
            for m in range(M):
                for j in range(J):
                    sp.dma_start(wh_raw[Q * j:Q * j + Q, m, :], wh_rows[m, j, :, :]).then_inc(wh_in[m], 16)
            load_x(0, 2)
            load_residual(0, 0)
            load_residual(0, 1)
            sp.wait_ge(h0_parts_ready, 1)
            for j in range(J):
                sp.dma_start(h0_units[Q * j:Q * j + Q, :, :],
                             h0_part[:, :, P * j:P * j + P]).then_inc(h0_moved, 16)
                sp.dma_start(h0_rel_all[Q * j:Q * j + Q, :], h0_rel[:, :]).then_inc(h0_moved, 16)
            for j in range(J):
                move_seeds(0, 0, j)
            load_x(0, 3)
            for j in range(J):
                move_seeds(0, 1, j)
            with sp.Fori(0, LOOPS) as i:
                for n in range(2):
                    block_dmas(i, n)
            for n in range(NBLK - 2 * LOOPS):
                block_dmas(LOOPS, n)
            for n in range(2):
                sp.wait_ge(out_stored[n], OUT_FREE + 16 * J * (NBLK // 2))

        @block.gpsimd
        def _(pool):
            pool.memset(zeros[:, :], 0.0).then_inc(const_ready, 1)
            pool.memset(ident[:, :], 0.0).then_inc(const_ready, 1)
            pool.wait_ge(const_ready, 2)
            pool.affine_select(out=ident[:, :], in_=ident[:, :], compare_op=ALU.not_equal, fill=1.0,
                               base=0, pattern=[[-1, P]], channel_multiplier=1).then_inc(const_ready, 1)
            for w in range(2):
                pool.wait_ge(w_max_ready, w + 1)
                pool.partition_all_reduce(w_top[:, w:w + 1], w_max1[:, w:w + 1], P,
                                          bass.bass_isa.ReduceOp.max).then_inc(w_top_ready, 1)
            pool.sem_inc(out_ready, H_FREE)

            def residual(i, s):
                n, r = s // TB, s % TB
                if r == 0:
                    pool.wait_ge(x_res_loaded[n % 2], 16 * J * uses(i, n))
                    pool.wait_ge(out_stored[n % 2], OUT_FREE + 16 * J * (uses(i, n) - 1))
                pool.wait_ge(h_ready, RING * i + s + 1)
                pool.tensor_tensor(out=out_buf[:, n % 2, r, :], in0=h[:, s % 2, :],
                                   in1=x_res[:, n % 2, r, :], op=ALU.add).then_inc(out_ready, 1)

            with pool.Fori(0, LOOPS) as i:
                for s in range(RING):
                    residual(i, s)
            for s in range(T - RING * LOOPS):
                residual(LOOPS, s)

        @block.scalar
        def _(act):
            def weight_hi(raw, part, w, count):
                act.wait_ge(w_scale_ready, w + 1)
                for k in range(count):
                    act.activation(part[:, HI, k, :, :].rearrange("p j (g c) -> p j g c", g=G),
                                   raw[:, k, :].rearrange("p (g j c) -> p j g c", g=G, j=J),
                                   ACT.Copy, scale=f32v(w_scale[:, w:w + 1])).then_inc(w_hi_ready, 1)

            def take_turned(i, n):
                if has(i, n):
                    act.wait_ge(x_turned, block_of(i, n) + 1)
                    if has(i, n - 2):
                        act.wait_ge(xp_done, TB * (block_of(i, n) - 1))
                    act.activation(xT[:, n % 2, :, :, :].rearrange("p a k c -> p (a k c)"),
                                   trp[:, :, :, :].rearrange("p a k c -> p (a k c)"),
                                   ACT.Copy).then_inc(xT_ready, 1)

            def seed(i, s):
                n, r = s // TB, s % TB
                if r == 0 or (isinstance(i, int) and i == 0 and s == 1):
                    act.wait_ge(seeds_moved[n % 2], 16 * TB * J * uses(i, n))
                act.activation(gates[s % BANKS][:, :], seeds[:, n % 2, r, :], ACT.Copy,
                               scale=seed_scale[:, :]).then_inc(seeded, 1)

            def step(i, s):
                u = s % 2
                bank = gates[s % BANKS]
                unscale = f32v(gate_unscale[:, :])
                act.wait_ge(gates_done, RING * i + s + 1)
                act.activation(if_act[:, u, :, :].rearrange("p a c -> p (a c)"), bank[:, 0:2 * P],
                               ACT.Sigmoid, scale=unscale).then_inc(if_ready, 1)
                act.activation(g_act[:, u, :], bank[:, 3 * P:4 * P], ACT.Tanh,
                               scale=unscale).then_inc(g_ready, 1)
                act.activation(o_act[:, u, :], bank[:, 2 * P:3 * P], ACT.Sigmoid,
                               scale=unscale).then_inc(o_ready, 1)
                act.wait_ge(c_ready, RING * i + s + 1)
                act.activation(tc[:, u, :], c[:, u, :], ACT.Tanh).then_inc(tc_ready, 1)
                if not isinstance(i, int) or RING * i + s + 2 < T:
                    seed(i, s + 2)
                if s % TB == TB - 1:
                    take_turned(i, s // TB + AHEAD_SPLIT)

            weight_hi(wx_raw, wx_part, 0, K)
            take_turned(0, 0)
            take_turned(0, 1)
            weight_hi(wh_raw, wh_part, 1, M)
            take_turned(0, 2)
            act.wait_ge(banks_open, 1)
            seed(0, 1)
            with act.Fori(0, LOOPS) as i:
                for s in range(RING):
                    step(i, s)
            for s in range(T - RING * LOOPS):
                step(LOOPS, s)

        @block.vector
        def _(dve):
            done = [0]

            def link(instruction):
                instruction.then_inc(small, 1)
                done[0] += 1
                dve.wait_ge(small, done[0])

            def scales(top, exp, scale, unscale):
                link(nc.vector.tensor_scalar(top, top, TINY, None, ALU.max))
                link(nc.vector.tensor_scalar(exp, top.bitcast(I32), 0x7F800000, None, ALU.bitwise_and))
                link(nc.vector.tensor_scalar(scale, exp, -1.0, float((HEAD + 2 * 127) * ONE_EXP),
                                             ALU.mult, ALU.add))
                link(nc.vector.tensor_scalar(unscale, exp, float(-HEAD * ONE_EXP), None, ALU.add))

            def weight_max(raw, arrived, w, count, transfers):
                for k in range(count):
                    dve.wait_ge(arrived[k], 16 * transfers)
                    ins = nc.vector.tensor_reduce(w_max[:, w, k:k + 1], raw[:, k, :], AX, ALU.max,
                                                  apply_absolute_value=True)
                    if k < count - 1:
                        ins.then_inc(small, 1)
                        done[0] += 1
                    else:
                        link(ins)
                if w == 0:
                    dve.wait_ge(bias_in, 16)
                nc.vector.tensor_reduce(w_max1[:, w:w + 1], w_max[:, w, :], AX, ALU.max)\
                  .then_inc(w_max_ready, 1)

            def weight_scales(w):
                dve.wait_ge(w_top_ready, w + 1)
                scales(w_top[:, w:w + 1], w_exp[:, w:w + 1], w_scale[:, w:w + 1],
                       w_unscale[:, w:w + 1])
                if w == 1:
                    link(nc.vector.tensor_scalar(seed_scale[:, :], f32v(w_scale[:, 1:2]), H_SCALE,
                                                 None, ALU.mult))
                    link(nc.vector.tensor_scalar(gate_unscale[:, :], w_exp[:, 1:2],
                                                 float(-2 * HEAD * ONE_EXP), None, ALU.add))
                dve.sem_inc(w_scale_ready, 1)

            def weight_lo(raw, part, w, count, ready):
                for k in range(count):
                    dve.wait_ge(w_hi_ready, w * K + k + 1)
                    by_gate = raw[:, k, :].rearrange("p (g j c) -> p j g c", g=G, j=J)
                    for j in range(J):
                        nc.vector.scalar_tensor_tensor(
                            out=part[:, LO, k, j, :].rearrange("p (g c) -> p g c", g=G),
                            in0=by_gate[:, j, :, :], scalar=f32v(w_scale[:, w:w + 1]),
                            in1=part[:, HI, k, j, :].rearrange("p (g c) -> p g c", g=G),
                            op0=ALU.mult, op1=ALU.subtract).then_inc(ready, 1)

            x_ops = [0]

            def x_scales(i, n):
                if not has(i, n):
                    return
                dve.wait_ge(x_in_loaded[n % 2], 16 * TB * uses(i, n))
                base = 6 * block_of(i, n)

                def x_link(instruction):
                    instruction.then_inc(x_max_ready, 1)
                    x_ops[0] += 1
                    dve.wait_ge(x_max_ready, base + x_ops[0])

                x_ops[0] = 0
                x_link(nc.vector.tensor_reduce(x_max[:, :], x_in[:, n % 2, :], AX, ALU.max,
                                               apply_absolute_value=True))
                x_link(nc.vector.tensor_scalar(x_max[:, :], x_max[:, :], TINY, None, ALU.max))
                x_link(nc.vector.tensor_scalar(x_exp[:, :], x_max[:, :].bitcast(I32), 0x7F800000, None,
                                               ALU.bitwise_and))
                x_link(nc.vector.tensor_scalar(x_scale[:, :], x_exp[:, :], -1.0,
                                               float((HEAD + 2 * 127) * ONE_EXP), ALU.mult, ALU.add))
                x_link(nc.vector.tensor_scalar(x_unscale[:, :], x_exp[:, :], float(-HEAD * ONE_EXP),
                                               None, ALU.add))
                x_link(nc.vector.tensor_scalar(xw_scale[:, n % 2:n % 2 + 1], f32v(x_unscale[:, :]),
                                               f32v(w_unscale[:, 0:1]), None, ALU.mult))

            def x_hi(i, n):
                if has(i, n):
                    nc.vector.tensor_scalar(x_part[:, n % 2, HI, :], x_in[:, n % 2, :],
                                            f32v(x_scale[:, :]), None, ALU.mult).then_inc(x_hi_ready, 1)

            def x_lo(i, n):
                if has(i, n):
                    dve.wait_ge(x_hi_ready, block_of(i, n) + 1)
                    nc.vector.scalar_tensor_tensor(
                        out=x_part[:, n % 2, LO, :], in0=x_in[:, n % 2, :], scalar=f32v(x_scale[:, :]),
                        in1=x_part[:, n % 2, HI, :], op0=ALU.mult,
                        op1=ALU.subtract).then_inc(x_part_ready, 1)

            def take_product(i, n, j):
                if not has(i, n):
                    return
                dve.wait_ge(xp_done, TB * block_of(i, n) + j + 1)
                if j == 0 and has(i, n - 1):
                    dve.wait_ge(seeds_moved[(n - 1) % 2], 16 * TB * J * uses(i, n - 1))
                nc.vector.scalar_tensor_tensor(
                    out=xw[:, j, :].rearrange("p (g c) -> p g c", g=G),
                    in0=xp[j % 2][:, :].rearrange("p (g c) -> p g c", g=G),
                    scalar=xw_scale[:, n % 2:n % 2 + 1],
                    in1=bias_all[:, :].rearrange("p (g j c) -> p j g c", g=G, j=J)[:, j, :, :],
                    op0=ALU.mult, op1=ALU.add).then_inc(xw_ready, 1)

            def step(i, s):
                u = s % 2
                now = RING * i + s + 1
                dve.wait_ge(if_ready, now)
                nc.vector.tensor_tensor(out=fc[:, :], in0=if_act[:, u, 1, :], in1=c[:, 1 - u, :],
                                        op=ALU.mult).then_inc(fc_ready, 1)
                dve.wait_ge(g_ready, now)
                nc.vector.tensor_tensor(out=ig[:, :], in0=if_act[:, u, 0, :], in1=g_act[:, u, :],
                                        op=ALU.mult).then_inc(ig_ready, 1)
                dve.wait_ge(fc_ready, now)
                dve.wait_ge(ig_ready, now)
                nc.vector.tensor_tensor(out=c[:, u, :], in0=fc[:, :], in1=ig[:, :],
                                        op=ALU.add).then_inc(c_ready, 1)
                dve.wait_ge(o_ready, now)
                dve.wait_ge(tc_ready, now)
                last = isinstance(i, int) and RING * i + s == T - 1
                if not last:
                    nc.vector.scalar_tensor_tensor(out=h_part[:, HI, :], in0=tc[:, u, :],
                                                   scalar=H_SCALE, in1=o_act[:, u, :], op0=ALU.mult,
                                                   op1=ALU.mult).then_inc(h_hi_ready, 1)
                    dve.wait_ge(h_hi_ready, now)
                    nc.vector.transpose(hT[:, 1 - u, HI, :, :].rearrange("p m b -> p (m b)"),
                                        h_part[:, HI, :]).then_inc(hT_hi_ready, 1)
                dve.wait_ge(out_ready, now)
                nc.vector.tensor_tensor(out=h[:, u, :], in0=tc[:, u, :], in1=o_act[:, u, :],
                                        op=ALU.mult).then_inc(h_ready, 1)
                if not last:
                    dve.wait_ge(h_ready, now)
                    nc.vector.scalar_tensor_tensor(out=h_part[:, LO, :], in0=h[:, u, :],
                                                   scalar=H_SCALE, in1=h_part[:, HI, :], op0=ALU.mult,
                                                   op1=ALU.subtract).then_inc(h_lo_ready, 1)
                    dve.wait_ge(h_lo_ready, now)
                    nc.vector.transpose(hT[:, 1 - u, LO, :, :].rearrange("p m b -> p (m b)"),
                                        h_part[:, LO, :]).then_inc(hT_lo_ready, 1)
                n, r = s // TB, s % TB
                take_product(i, n + AHEAD_PRODUCT, r)
                if r == 0:
                    x_scales(i, n + AHEAD_SPLIT)
                if r == 1:
                    x_hi(i, n + AHEAD_SPLIT)
                if r == 2:
                    x_lo(i, n + AHEAD_SPLIT)

            def x_split(n):
                x_scales(0, n)
                x_hi(0, n)
                x_lo(0, n)

            nc.vector.memset(c[:, 1, :], 0.0)
            dve.wait_ge(h0_loaded, 16)
            link(nc.vector.tensor_reduce(h0_max[:, :], h0_in[:, :], AX, ALU.max,
                                         apply_absolute_value=True))
            scales(h0_max[:, :], h0_exp[:, :], h0_scale[:, :], h0_unscale[:, :])
            link(nc.vector.tensor_scalar(h0_rel[:, :], f32v(h0_unscale[:, :]), H_SCALE, None, ALU.mult))
            link(nc.vector.tensor_scalar(h0_part[:, HI, :], h0_in[:, :], f32v(h0_scale[:, :]), None,
                                         ALU.mult))
            nc.vector.scalar_tensor_tensor(
                out=h0_part[:, LO, :], in0=h0_in[:, :], scalar=f32v(h0_scale[:, :]),
                in1=h0_part[:, HI, :], op0=ALU.mult, op1=ALU.subtract).then_inc(h0_parts_ready, 1)
            weight_max(wx_raw, wx_in, 0, K, 1)
            weight_scales(0)
            x_split(0)
            weight_lo(wx_raw, wx_part, 0, K, wx_ready)
            x_split(1)
            for j in range(J):
                take_product(0, 0, j)
            x_split(2)
            weight_max(wh_raw, wh_in, 1, M, J)
            weight_scales(1)
            for j in range(J):
                take_product(0, 1, j)
            weight_lo(wh_raw, wh_part, 1, M, wh_ready)
            dve.wait_ge(h0_moved, 16 * 2 * J)
            nc.vector.transpose(hT[:, 0, HI, :, :].rearrange("p m b -> p (m b)"),
                                h0_units[:, HI, :]).then_inc(hT_hi_ready, 1)
            nc.vector.transpose(hT[:, 0, LO, :, :].rearrange("p m b -> p (m b)"),
                                h0_units[:, LO, :]).then_inc(hT_lo_ready, 1)
            dve.wait_ge(seeds_moved[0], 16 * TB * J)
            link(nc.vector.tensor_scalar(seed0[:, :], seeds[:, 0, 0, :], seed_scale[:, :], None,
                                         ALU.mult))
            dve.wait_ge(h0_product, 1)
            link(nc.vector.tensor_scalar(h0_prod[:, :], gates[0][:, :], h0_rel_all[:, :], None,
                                         ALU.mult))
            nc.vector.tensor_tensor(out=gates[0][:, :], in0=h0_prod[:, :], in1=seed0[:, :],
                                    op=ALU.add).then_inc(gates_done, 1)
            with dve.Fori(0, LOOPS) as i:
                for s in range(RING):
                    step(i, s)
            for s in range(T - RING * LOOPS):
                step(LOOPS, s)

        @block.tensor
        def _(pe):
            def recurrent(bank, half, start, before_lo):
                for a, w in PRODUCTS:
                    if a == LO:
                        before_lo()
                    for m in range(M):
                        for j in range(J):
                            last = nc.tensor.matmul(
                                bank[Q * j:Q * j + Q, :], hT[:, half, a, m, :],
                                wh_part[:, w, m, j, :], start=start and (a, w, m) == (HI, HI, 0),
                                stop=(a, w, m) == (LO, HI, M - 1), skip_group_check=True)
                return last

            def product(i, n, j):
                if not has(i, n):
                    return
                if j == 0:
                    pe.wait_ge(xT_ready, block_of(i, n) + 1)
                if not isinstance(i, int) or i > 0 or TB * n + j >= 2:
                    pe.wait_ge(xw_ready, TB * block_of(i, n) + j - 1)
                for a, w in PRODUCTS:
                    for k in range(K):
                        last = nc.tensor.matmul(
                            xp[j % 2][:, :], xT[:, n % 2, a, k, :], wx_part[:, w, k, j, :],
                            start=(a, w, k) == (HI, HI, 0), stop=(a, w, k) == (LO, HI, K - 1))
                last.then_inc(xp_done, 1)

            def turn(i, n):
                if not has(i, n):
                    return
                pe.wait_ge(x_part_ready, block_of(i, n) + 1)
                if has(i, n - 1):
                    pe.wait_ge(xT_ready, block_of(i, n))
                for a in (HI, LO):
                    for k in range(K):
                        last = nc.tensor.transpose(trp[:, a, k, :],
                                                   x_part[:, n % 2, a, P * k:P * k + P], ident[:, :])
                last.then_inc(x_turned, 1)

            def step(i, s):
                n, r = s // TB, s % TB
                product(i, n + AHEAD_PRODUCT, r)
                if r == TB - 1:
                    turn(i, n + AHEAD_SPLIT)
                if isinstance(i, int) and RING * i + s == T - 1:
                    return
                nxt = RING * i + s + 1
                pe.wait_ge(seeded, nxt)
                pe.wait_ge(hT_hi_ready, nxt + 1)
                recurrent(gates[(s + 1) % BANKS], (s + 1) % 2, False,
                          lambda: pe.wait_ge(hT_lo_ready, nxt + 1)).then_inc(gates_done, 1)

            pe.wait_ge(const_ready, 3)
            for n in range(1, BANKS):
                last = nc.tensor.matmul(gates[n][:, :], ident[:, :], zeros[:, :], start=True, stop=True)
            last.then_inc(banks_open, 1)
            turn(0, 0)
            pe.wait_ge(wx_ready, K * J)
            turn(0, 1)
            for j in range(J):
                product(0, 0, j)
            turn(0, 2)
            for j in range(J):
                product(0, 1, j)
            pe.wait_ge(wh_ready, M * J)
            pe.wait_ge(hT_hi_ready, 1)
            recurrent(gates[0], 0, True, lambda: pe.wait_ge(hT_lo_ready, 1)).then_inc(h0_product, 1)
            with pe.Fori(0, LOOPS) as i:
                for s in range(RING):
                    step(i, s)
            for s in range(T - RING * LOOPS):
                step(LOOPS, s)


_INS = ['x', 'cond_1024', 'L0_cond_Wx', 'L0_cond_Wh', 'L0_cond_b']
_OUTS = [((32, 128, 512), 'float32')]


def kernel(**inputs):
    import numpy as _np
    import concourse.bacc as _bacc
    from concourse import mybir as _mybir
    from concourse.bass_utils import run_bass_kernel_spmd as _run

    nc = _bacc.Bacc("TRN2", target_bir_lowering=False, num_devices=1)
    arrays, args = {}, []
    for name in _INS:
        a = _np.ascontiguousarray(inputs[name])
        arrays[f"in_{name}_dram"] = a
        args.append(nc.dram_tensor(f"in_{name}_dram", a.shape, _mybir.dt.from_np(a.dtype), kind="ExternalInput").ap())
    for i, (shape, dtype) in enumerate(_OUTS):
        dt = _mybir.dt.from_np(_np.dtype(dtype))
        args.append(nc.dram_tensor(f"out_{i}_dram", shape, dt, kind="ExternalOutput").ap())
    lstm_kernel(nc, *args)
    r = _run(nc, [arrays], core_ids=[0])
    got = tuple(r.results[0][f"out_{i}_dram"] for i in range(len(_OUTS)))
    return got[0]
```

```python
import concourse.bass as bass
from concourse import mybir
from contextlib import ExitStack


F32 = mybir.dt.float32
F16 = mybir.dt.float16
I32 = mybir.dt.int32
ALU = mybir.AluOpType
ACT = mybir.ActivationFunctionType
AX = mybir.AxisListType.X

P = 128
Q = 32
TB = 4
RING = 8
BANKS = 4
AHEAD_PRODUCT = 6
AHEAD_TURN = 2
AHEAD_SPLIT = 3
AHEAD_LOAD = 4
HEAD = 14
H_SCALE = float(2 ** HEAD)
TINY = 2.0 ** -60
ONE_EXP = 1 << 23
SUM_SHRINK = 14
WARM = 7
HI, LO = 0, 1
OUT_FREE = 16
H_FREE = 2
PRODUCTS = ((HI, HI), (HI, LO), (LO, HI))


def lstm_kernel(nc: bass.Bass, x: bass.AP, h0: bass.AP, wx: bass.AP, wh: bass.AP, bias: bass.AP,
                out: bass.AP):
    B, T, D = x.shape
    H = h0.shape[1]
    G = wx.shape[1] // H
    K = D // P
    J = H // P
    M = P // Q
    GC = G * P
    NBLK = T // TB
    LOOPS = (NBLK - AHEAD_LOAD) // 2
    assert B == Q and D == H and J * B == P and TB * B == P and G == 4 and GC == 512

    x_rows = x.rearrange("b (q t) d -> q t b d", t=TB)
    x_units = x.rearrange("b (q t) (j c) -> q j b t c", t=TB, j=J)
    out_units = out.rearrange("b (q t) (j c) -> q j b t c", t=TB, j=J)
    wx_rows = wx.rearrange("(k p) n -> k p n", p=P)
    wh_rows = wh.rearrange("(j m x) n -> m j x n", m=M, x=Q)

    ctx = ExitStack()
    with ctx:
        def sb(name, shape, dt):
            return ctx.enter_context(nc.sbuf_tensor(name, shape, dt))

        def pb(name, shape, dt):
            return ctx.enter_context(nc.psum_tensor(name, shape, dt))

        def sem(name):
            return ctx.enter_context(nc.semaphore(name))

        wx_raw = sb("wx_raw", [P, K, G * H], F32)
        wh_raw = sb("wh_raw", [P, M, G * H], F32)
        wx_part = sb("wx_part", [P, 2, K, J, GC], F16)
        wh_part = sb("wh_part", [P, 2, M, J, GC], F16)
        bias_row = sb("bias_row", [1, G * H], F32)
        bias_all = sb("bias_all", [P, G * H], F32)
        w_max = sb("w_max", [P, 2, K], F32)
        w_max1 = sb("w_max1", [P, 2], F32)
        w_top = sb("w_top", [P, 2], F32)
        w_exp = sb("w_exp", [P, 2], I32)
        w_scale = sb("w_scale", [P, 2], I32)
        wx_unscale = sb("wx_unscale", [P, 1], I32)

        seed_scale = sb("seed_scale", [P, 1], F32)
        gate_unscale = sb("gate_unscale", [P, 1], I32)
        ident = sb("ident", [P, P], F16)
        zeros = sb("zeros", [P, GC], F16)

        x_in = sb("x_in", [P, 2, D], F32)
        x_max = sb("x_max", [P, 1], F32)
        x_exp = sb("x_exp", [P, 1], I32)
        x_scale = sb("x_scale", [P, 1], I32)
        x_unscale = sb("x_unscale", [P, 2], I32)
        xw_scale = sb("xw_scale", [P, 2], F32)
        x_part = sb("x_part", [P, 2, 2, D], F16)
        xT = sb("xT", [P, 2, 2, K, P], F16)
        xw = sb("xw", [P, J, GC], F32)
        seeds = sb("seeds", [P, 2, TB, GC], F32)

        h0_in = sb("h0_in", [B, H], F32)
        h0_max = sb("h0_max", [B, 1], F32)
        h0_exp = sb("h0_exp", [B, 1], I32)
        h0_scale = sb("h0_scale", [B, 1], I32)
        h0_unscale = sb("h0_unscale", [B, 1], I32)
        h0_rel = sb("h0_rel", [B, 1], F32)
        h0_part = sb("h0_part", [B, 2, H], F16)
        h0_units = sb("h0_units", [P, 2, P], F16)
        h0_rel_all = sb("h0_rel_all", [P, 1], F32)
        seed0 = sb("seed0", [P, GC], F32)

        if_act = sb("if_act", [P, 2, 2, P], F32)
        g_act = sb("g_act", [P, 2, P], F32)
        o_act = sb("o_act", [P, 2, P], F32)
        fc = sb("fc", [P, P], F32)
        ig = sb("ig", [P, P], F32)
        c = sb("c", [P, 2, P], F32)
        tc = sb("tc", [P, 2, P], F32)
        h = sb("h", [P, 2, P], F32)
        h_part = sb("h_part", [P, 2, P], F16)
        hT = sb("hT", [P, 2, 2, M, B], F16)
        x_res = sb("x_res", [P, 2, TB, P], F32)
        out_buf = sb("out_buf", [P, 2, TB, P], F32)

        gates = [pb(f"gates{n}", [P, GC], F32) for n in range(BANKS)]
        xp = [pb(f"xp{n}", [P, GC], F32) for n in range(2)]
        trp = pb("trp", [P, 2, K, P], F16)

        wx_in = [sem(f"wx_in{k}") for k in range(K)]
        wh_in = [sem(f"wh_in{k}") for k in range(M)]
        bias_in = sem("bias_in")
        bias_ready = sem("bias_ready")
        h0_loaded = sem("h0_loaded")
        h0_moved = sem("h0_moved")
        x_in_loaded = [sem(f"x_in_loaded{n}") for n in range(2)]
        x_res_loaded = [sem(f"x_res_loaded{n}") for n in range(2)]
        seeds_moved = [sem(f"seeds_moved{n}") for n in range(2)]
        out_stored = [sem(f"out_stored{n}") for n in range(2)]
        const_ready = sem("const_ready")
        w_max_ready = sem("w_max_ready")
        w_top_ready = sem("w_top_ready")
        w_scale_ready = sem("w_scale_ready")
        wh_sums_ready = sem("wh_sums_ready")
        gate_scales_ready = sem("gate_scales_ready")
        w_hi_ready = sem("w_hi_ready")
        wx_ready = sem("wx_ready")
        wh_ready = sem("wh_ready")
        small = sem("small")
        banks_open = sem("banks_open")
        h0_parts_ready = sem("h0_parts_ready")
        h0_product = sem("h0_product")
        seed0_ready = sem("seed0_ready")
        x_max_ready = sem("x_max_ready")
        xw_scale_ready = sem("xw_scale_ready")
        x_hi_ready = sem("x_hi_ready")
        x_part_ready = sem("x_part_ready")
        x_turned = sem("x_turned")
        xT_ready = sem("xT_ready")
        xp_done = sem("xp_done")
        xw_ready = sem("xw_ready")
        seeded = sem("seeded")
        gates_done = sem("gates_done")
        if_ready = sem("if_ready")
        g_ready = sem("g_ready")
        ig_ready = sem("ig_ready")
        c_ready = sem("c_ready")
        tc_ready = sem("tc_ready")
        h_hi_ready = sem("h_hi_ready")
        hT_hi_ready = sem("hT_hi_ready")
        h_ready = sem("h_ready")
        h_lo_ready = sem("h_lo_ready")
        hT_lo_ready = sem("hT_lo_ready")
        out_ready = sem("out_ready")

        f32v = lambda t: t.bitcast(F32)
        has = lambda i, n: not isinstance(i, int) or 0 <= 2 * i + n < NBLK
        block_of = lambda i, n: 2 * i + n
        uses = lambda i, n: i + n // 2 + 1

        block = ctx.enter_context(nc.Block())

        @block.sync
        def _(sp):
            def load_x(i, n):
                if has(i, n):
                    if has(i, n - 2):
                        sp.wait_ge(x_part_ready, block_of(i, n - 2) + 1)
                    for t in range(TB):
                        sp.dma_start(x_in[Q * t:Q * t + Q, n % 2, :],
                                     x_rows[block_of(i, n), t, :, :]).then_inc(x_in_loaded[n % 2], 16)

            def load_residual(i, n):
                if has(i, n):
                    for j in range(J):
                        sp.dma_start(x_res[Q * j:Q * j + Q, n % 2, :, :],
                                     x_units[block_of(i, n), j, :, :, :]).then_inc(x_res_loaded[n % 2], 16)

            def move_seeds(i, n, j):
                if has(i, n):
                    sp.wait_ge(xw_ready, TB * block_of(i, n) + j + 1)
                    for t in range(TB):
                        sp.dma_start(seeds[Q * j:Q * j + Q, n % 2, t, :],
                                     xw[Q * t:Q * t + Q, j, :]).then_inc(seeds_moved[n % 2], 16)

            def block_dmas(i, n):
                load_x(i, n + AHEAD_LOAD)
                for r in range(TB):
                    ahead, j = divmod(TB * n + r + AHEAD_PRODUCT, J)
                    if j == 0 and has(i, ahead):
                        sp.wait_ge(seeded, TB * block_of(i, ahead - 2) + TB - 1)
                    move_seeds(i, ahead, j)
                sp.wait_ge(out_ready, H_FREE + TB * block_of(i, n) + TB)
                for j in range(J):
                    sp.dma_start(out_units[block_of(i, n), j, :, :, :],
                                 out_buf[Q * j:Q * j + Q, n % 2, :, :]).then_inc(out_stored[n % 2], 16)
                load_residual(i, n + 2)

            for n in range(2):
                sp.sem_inc(out_stored[n], OUT_FREE)
            load_x(0, 0)
            sp.dma_start(h0_in[:, :], h0).then_inc(h0_loaded, 16)
            sp.dma_start(bias_row[:, :], bias.rearrange("(a n) -> a n", a=1)).then_inc(bias_in, 16)
            for k in range(K):
                sp.dma_start(wx_raw[:, k, :], wx_rows[k, :, :]).then_inc(wx_in[k], 16)
            load_x(0, 1)
            for m in range(M):
                for j in range(J):
                    sp.dma_start(wh_raw[Q * j:Q * j + Q, m, :], wh_rows[m, j, :, :]).then_inc(wh_in[m], 16)
            load_x(0, 2)
            load_x(0, 3)
            sp.wait_ge(h0_parts_ready, 1)
            for j in range(J):
                sp.dma_start(h0_units[Q * j:Q * j + Q, :, :],
                             h0_part[:, :, P * j:P * j + P]).then_inc(h0_moved, 16)
                sp.dma_start(h0_rel_all[Q * j:Q * j + Q, :], h0_rel[:, :]).then_inc(h0_moved, 16)
            load_residual(0, 0)
            load_residual(0, 1)
            for n in range(AHEAD_PRODUCT):
                move_seeds(0, *divmod(n, J))
            with sp.Fori(0, LOOPS) as i:
                for n in range(2):
                    block_dmas(i, n)
            for n in range(NBLK - 2 * LOOPS):
                block_dmas(LOOPS, n)
            for n in range(2):
                sp.wait_ge(out_stored[n], OUT_FREE + 16 * J * (NBLK // 2))

        @block.gpsimd
        def _(pool):
            pool.memset(zeros[:, :], 0.0).then_inc(const_ready, 1)
            pool.memset(ident[:, :], 0.0).then_inc(const_ready, 1)
            pool.wait_ge(const_ready, 2)
            pool.affine_select(out=ident[:, :], in_=ident[:, :], compare_op=ALU.not_equal, fill=1.0,
                               base=0, pattern=[[-1, P]], channel_multiplier=1).then_inc(const_ready, 1)
            pool.wait_ge(bias_in, 16)
            pool.partition_broadcast(bias_all[:, :], bias_row[:, :]).then_inc(bias_ready, 1)
            for w in range(2):
                pool.wait_ge(w_max_ready, w + 1)
                pool.partition_all_reduce(w_top[:, w:w + 1], w_max1[:, w:w + 1], P,
                                          bass.bass_isa.ReduceOp.max).then_inc(w_top_ready, 1)
            pool.sem_inc(out_ready, H_FREE)

            def residual(i, s):
                n, r = s // TB, s % TB
                if r == 0:
                    pool.wait_ge(x_res_loaded[n % 2], 16 * J * uses(i, n))
                    pool.wait_ge(out_stored[n % 2], OUT_FREE + 16 * J * (uses(i, n) - 1))
                pool.wait_ge(h_ready, RING * i + s + 1)
                pool.tensor_tensor(out=out_buf[:, n % 2, r, :], in0=h[:, s % 2, :],
                                   in1=x_res[:, n % 2, r, :], op=ALU.add).then_inc(out_ready, 1)

            with pool.Fori(0, LOOPS) as i:
                for s in range(RING):
                    residual(i, s)
            for s in range(T - RING * LOOPS):
                residual(LOOPS, s)

        @block.scalar
        def _(act):
            def weight_hi(raw, part, w, count, chunks):
                act.wait_ge(w_scale_ready, w + 1)
                for j in chunks:
                    for k in range(count):
                        by_gate = raw[:, k, :].rearrange("p (g j c) -> p j g c", g=G, j=J)
                        act.activation(part[:, HI, k, j, :].rearrange("p (g c) -> p g c", g=G),
                                       by_gate[:, j, :, :], ACT.Copy,
                                       scale=f32v(w_scale[:, w:w + 1])).then_inc(w_hi_ready, 1)

            def wh_sums():
                for m in range(M - 1):
                    act.wait_ge(wh_in[m], 16 * J)
                    act.activation(wh_part[:, LO, m, :, :].rearrange("p j c -> p (j c)"),
                                   wh_raw[:, m, :], ACT.Abs, scale=2.0 ** -SUM_SHRINK,
                                   accum_out=w_max[:, 1, m:m + 1]).then_inc(wh_sums_ready, 1)

            def take_turned(i, n):
                if has(i, n):
                    act.wait_ge(x_turned, block_of(i, n) + 1)
                    if has(i, n - 2):
                        act.wait_ge(xp_done, TB * (block_of(i, n) - 1))
                    act.activation(xT[:, n % 2, :, :, :].rearrange("p a k c -> p (a k c)"),
                                   trp[:, :, :, :].rearrange("p a k c -> p (a k c)"),
                                   ACT.Copy).then_inc(xT_ready, 1)

            def seed(i, s):
                n, r = s // TB, s % TB
                if r == 0 or (isinstance(i, int) and i == 0 and s == 1):
                    act.wait_ge(seeds_moved[n % 2], 16 * TB * J * uses(i, n))
                act.activation(gates[s % BANKS][:, :], seeds[:, n % 2, r, :], ACT.Copy,
                               scale=seed_scale[:, :]).then_inc(seeded, 1)

            def step(i, s):
                u = s % 2
                bank = gates[s % BANKS]
                unscale = f32v(gate_unscale[:, :])
                act.wait_ge(gates_done, RING * i + s + 1)
                act.activation(if_act[:, u, :, :].rearrange("p a c -> p (a c)"), bank[:, 0:2 * P],
                               ACT.Sigmoid, scale=unscale).then_inc(if_ready, 1)
                act.activation(g_act[:, u, :], bank[:, 3 * P:4 * P], ACT.Tanh,
                               scale=unscale).then_inc(g_ready, 1)
                act.activation(o_act[:, u, :], bank[:, 2 * P:3 * P], ACT.Sigmoid,
                               scale=unscale)
                act.wait_ge(c_ready, RING * i + s + 1)
                act.activation(tc[:, u, :], c[:, u, :], ACT.Tanh).then_inc(tc_ready, 1)
                if not isinstance(i, int) or RING * i + s + 2 < T:
                    seed(i, s + 2)
                if s % TB == 1:
                    take_turned(i, s // TB + AHEAD_TURN)

            take_turned(0, 0)
            weight_hi(wx_raw, wx_part, 0, K, range(1))
            take_turned(0, 1)
            weight_hi(wx_raw, wx_part, 0, K, range(1, J))
            wh_sums()
            weight_hi(wh_raw, wh_part, 1, M, range(J))
            act.wait_ge(gate_scales_ready, 1)
            act.wait_ge(banks_open, 1)
            seed(0, 1)
            with act.Fori(0, LOOPS) as i:
                for s in range(RING):
                    step(i, s)
            for s in range(T - RING * LOOPS):
                step(LOOPS, s)

        @block.vector
        def _(dve):
            done = [0]

            def link(instruction):
                instruction.then_inc(small, 1)
                done[0] += 1
                dve.wait_ge(small, done[0])

            def scales(top, exp, scale, unscale, shrunk=0):
                link(nc.vector.tensor_scalar(top, top, TINY, None, ALU.max))
                link(nc.vector.tensor_scalar(exp, top.bitcast(I32), 0x7F800000, None, ALU.bitwise_and))
                link(nc.vector.tensor_scalar(scale, exp, -1.0,
                                             float((HEAD - shrunk + 2 * 127) * ONE_EXP),
                                             ALU.mult, ALU.add))
                if unscale is not None:
                    link(nc.vector.tensor_scalar(unscale, exp, float((shrunk - HEAD) * ONE_EXP),
                                                 None, ALU.add))

            def wx_max(k):
                dve.wait_ge(wx_in[k], 16)
                link(nc.vector.tensor_reduce(w_max[:, 0, k:k + 1], wx_raw[:, k, :], AX, ALU.max,
                                             apply_absolute_value=True))

            def wh_last_max():
                dve.wait_ge(wh_in[M - 1], 16 * J)
                link(nc.vector.tensor_reduce(w_max[:, 1, M - 1:M], wh_raw[:, M - 1, :], AX, ALU.max,
                                             apply_absolute_value=True))
                link(nc.vector.tensor_scalar(w_max[:, 1, M - 1:M], w_max[:, 1, M - 1:M],
                                             2.0 ** -SUM_SHRINK, None, ALU.mult))

            def w_max_of_tiles(w):
                nc.vector.tensor_reduce(w_max1[:, w:w + 1], w_max[:, w, :], AX, ALU.max)\
                  .then_inc(w_max_ready, 1)

            def weight_scales(w):
                dve.wait_ge(w_top_ready, w + 1)
                if w == 0:
                    scales(w_top[:, 0:1], w_exp[:, 0:1], w_scale[:, 0:1], wx_unscale[:, :])
                else:
                    scales(w_top[:, 1:2], w_exp[:, 1:2], w_scale[:, 1:2], None, SUM_SHRINK)
                dve.sem_inc(w_scale_ready, 1)
                if w == 1:
                    link(nc.vector.tensor_scalar(seed_scale[:, :], f32v(w_scale[:, 1:2]), H_SCALE,
                                                 None, ALU.mult))
                    nc.vector.tensor_scalar(gate_unscale[:, :], w_exp[:, 1:2],
                                            float((SUM_SHRINK - 2 * HEAD) * ONE_EXP), None,
                                            ALU.add).then_inc(gate_scales_ready, 1)

            def weight_lo(raw, part, w, j, count, ready):
                for k in range(count):
                    dve.wait_ge(w_hi_ready, (w * J + j) * K + k + 1)
                    by_gate = raw[:, k, :].rearrange("p (g j c) -> p j g c", g=G, j=J)
                    last = nc.vector.scalar_tensor_tensor(
                        out=part[:, LO, k, j, :].rearrange("p (g c) -> p g c", g=G),
                        in0=by_gate[:, j, :, :], scalar=f32v(w_scale[:, w:w + 1]),
                        in1=part[:, HI, k, j, :].rearrange("p (g c) -> p g c", g=G),
                        op0=ALU.mult, op1=ALU.subtract)
                last.then_inc(ready, 1)

            x_ops = [0]

            def x_scales(i, n):
                if not has(i, n):
                    return
                dve.wait_ge(x_in_loaded[n % 2], 16 * TB * uses(i, n))
                base = 5 * block_of(i, n)

                def x_link(instruction):
                    instruction.then_inc(x_max_ready, 1)
                    x_ops[0] += 1
                    dve.wait_ge(x_max_ready, base + x_ops[0])

                x_ops[0] = 0
                x_link(nc.vector.tensor_reduce(x_max[:, :], x_in[:, n % 2, :], AX, ALU.max,
                                               apply_absolute_value=True))
                x_link(nc.vector.tensor_scalar(x_max[:, :], x_max[:, :], TINY, None, ALU.max))
                x_link(nc.vector.tensor_scalar(x_exp[:, :], x_max[:, :].bitcast(I32), 0x7F800000, None,
                                               ALU.bitwise_and))
                x_link(nc.vector.tensor_scalar(x_scale[:, :], x_exp[:, :], -1.0,
                                               float((HEAD + 2 * 127) * ONE_EXP), ALU.mult, ALU.add))
                x_link(nc.vector.tensor_scalar(x_unscale[:, n % 2:n % 2 + 1], x_exp[:, :], float(-HEAD * ONE_EXP),
                                               None, ALU.add))

            def x_hi(i, n):
                if has(i, n):
                    nc.vector.tensor_scalar(x_part[:, n % 2, HI, :], x_in[:, n % 2, :],
                                            f32v(x_scale[:, :]), None, ALU.mult).then_inc(x_hi_ready, 1)

            def x_lo(i, n):
                if has(i, n):
                    dve.wait_ge(x_hi_ready, block_of(i, n) + 1)
                    nc.vector.scalar_tensor_tensor(
                        out=x_part[:, n % 2, LO, :], in0=x_in[:, n % 2, :], scalar=f32v(x_scale[:, :]),
                        in1=x_part[:, n % 2, HI, :], op0=ALU.mult,
                        op1=ALU.subtract).then_inc(x_part_ready, 1)

            def take_product(i, n, j):
                if not has(i, n):
                    return
                if j == 0:
                    nc.vector.tensor_scalar(xw_scale[:, n % 2:n % 2 + 1], f32v(x_unscale[:, n % 2:n % 2 + 1]),
                                            f32v(wx_unscale[:, :]), None, ALU.mult)\
                      .then_inc(xw_scale_ready, 1)
                    dve.wait_ge(xw_scale_ready, block_of(i, n) + 1)
                dve.wait_ge(xp_done, TB * block_of(i, n) + j + 1)
                if j == 0 and has(i, n - 1):
                    dve.wait_ge(seeds_moved[(n - 1) % 2], 16 * TB * J * uses(i, n - 1))
                nc.vector.scalar_tensor_tensor(
                    out=xw[:, j, :].rearrange("p (g c) -> p g c", g=G),
                    in0=xp[j % 2][:, :].rearrange("p (g c) -> p g c", g=G),
                    scalar=xw_scale[:, n % 2:n % 2 + 1],
                    in1=bias_all[:, :].rearrange("p (g j c) -> p j g c", g=G, j=J)[:, j, :, :],
                    op0=ALU.mult, op1=ALU.add).then_inc(xw_ready, 1)

            def step(i, s):
                u = s % 2
                now = RING * i + s + 1
                dve.wait_ge(if_ready, now)
                nc.vector.tensor_tensor(out=fc[:, :], in0=if_act[:, u, 1, :], in1=c[:, 1 - u, :],
                                        op=ALU.mult)
                dve.wait_ge(g_ready, now)
                nc.vector.tensor_tensor(out=ig[:, :], in0=if_act[:, u, 0, :], in1=g_act[:, u, :],
                                        op=ALU.mult).then_inc(ig_ready, 1)
                dve.wait_ge(ig_ready, now)
                nc.vector.tensor_tensor(out=c[:, u, :], in0=fc[:, :], in1=ig[:, :],
                                        op=ALU.add).then_inc(c_ready, 1)
                dve.wait_ge(tc_ready, now)
                last = isinstance(i, int) and RING * i + s == T - 1
                if not last:
                    nc.vector.scalar_tensor_tensor(out=h_part[:, HI, :], in0=tc[:, u, :],
                                                   scalar=H_SCALE, in1=o_act[:, u, :], op0=ALU.mult,
                                                   op1=ALU.mult).then_inc(h_hi_ready, 1)
                    dve.wait_ge(h_hi_ready, now)
                    nc.vector.transpose(hT[:, 1 - u, HI, :, :].rearrange("p m b -> p (m b)"),
                                        h_part[:, HI, :]).then_inc(hT_hi_ready, 1)
                dve.wait_ge(out_ready, now)
                nc.vector.tensor_tensor(out=h[:, u, :], in0=tc[:, u, :], in1=o_act[:, u, :],
                                        op=ALU.mult).then_inc(h_ready, 1)
                if not last:
                    dve.wait_ge(h_ready, now)
                    nc.vector.scalar_tensor_tensor(out=h_part[:, LO, :], in0=h[:, u, :],
                                                   scalar=H_SCALE, in1=h_part[:, HI, :], op0=ALU.mult,
                                                   op1=ALU.subtract).then_inc(h_lo_ready, 1)
                    dve.wait_ge(h_lo_ready, now)
                    nc.vector.transpose(hT[:, 1 - u, LO, :, :].rearrange("p m b -> p (m b)"),
                                        h_part[:, LO, :]).then_inc(hT_lo_ready, 1)
                n, r = s // TB, s % TB
                take_product(i, *divmod(s + AHEAD_PRODUCT, J))
                if r == 0:
                    x_hi(i, n + AHEAD_SPLIT)
                if r == 1:
                    x_lo(i, n + AHEAD_SPLIT)
                if r == 3:
                    x_scales(i, n + AHEAD_SPLIT + 1)

            def x_split(n):
                x_hi(0, n)
                x_lo(0, n)

            nc.vector.memset(c[:, 1, :], 0.0)
            dve.wait_ge(h0_loaded, 16)
            link(nc.vector.tensor_reduce(h0_max[:, :], h0_in[:, :], AX, ALU.max,
                                         apply_absolute_value=True))
            scales(h0_max[:, :], h0_exp[:, :], h0_scale[:, :], h0_unscale[:, :])
            link(nc.vector.tensor_scalar(h0_rel[:, :], f32v(h0_unscale[:, :]), H_SCALE, None, ALU.mult))
            link(nc.vector.tensor_scalar(h0_part[:, HI, :], h0_in[:, :], f32v(h0_scale[:, :]), None,
                                         ALU.mult))
            nc.vector.scalar_tensor_tensor(
                out=h0_part[:, LO, :], in0=h0_in[:, :], scalar=f32v(h0_scale[:, :]),
                in1=h0_part[:, HI, :], op0=ALU.mult, op1=ALU.subtract).then_inc(h0_parts_ready, 1)
            x_scales(0, 0)
            x_split(0)
            for k in range(K):
                wx_max(k)
            w_max_of_tiles(0)
            x_scales(0, 1)
            weight_scales(0)
            x_split(1)
            dve.wait_ge(bias_ready, 1)
            for j in range(J):
                weight_lo(wx_raw, wx_part, 0, j, K, wx_ready)
            take_product(0, 0, 0)
            take_product(0, 0, 1)
            wh_last_max()
            dve.wait_ge(wh_sums_ready, M - 1)
            w_max_of_tiles(1)
            weight_scales(1)
            x_scales(0, 2)
            dve.wait_ge(h0_moved, 16 * 2 * J)
            nc.vector.transpose(hT[:, 0, HI, :, :].rearrange("p m b -> p (m b)"),
                                h0_units[:, HI, :]).then_inc(hT_hi_ready, 1)
            nc.vector.transpose(hT[:, 0, LO, :, :].rearrange("p m b -> p (m b)"),
                                h0_units[:, LO, :]).then_inc(hT_lo_ready, 1)
            x_split(2)
            for j in range(J):
                weight_lo(wh_raw, wh_part, 1, j, M, wh_ready)
                if j < 2:
                    take_product(0, 0, 2 + j)
            for j in range(AHEAD_PRODUCT - J):
                take_product(0, 1, j)
            dve.wait_ge(seeds_moved[0], 16 * TB * J)
            nc.vector.tensor_scalar(seed0[:, :], seeds[:, 0, 0, :], seed_scale[:, :], None,
                                    ALU.mult).then_inc(seed0_ready, 1)
            dve.wait_ge(x_part_ready, 3)
            x_scales(0, 3)
            dve.wait_ge(seed0_ready, 1)
            dve.wait_ge(h0_product, 1)
            nc.vector.scalar_tensor_tensor(out=gates[0][:, :], in0=gates[0][:, :],
                                           scalar=h0_rel_all[:, :], in1=seed0[:, :], op0=ALU.mult,
                                           op1=ALU.add).then_inc(gates_done, 1)
            with dve.Fori(0, LOOPS) as i:
                for s in range(RING):
                    step(i, s)
            for s in range(T - RING * LOOPS):
                step(LOOPS, s)

        @block.tensor
        def _(pe):
            def recurrent(bank, half, start, before_lo):
                for a, w in PRODUCTS:
                    if a == LO:
                        before_lo()
                    for m in range(M):
                        for j in range(J):
                            last = nc.tensor.matmul(
                                bank[Q * j:Q * j + Q, :], hT[:, half, a, m, :],
                                wh_part[:, w, m, j, :], start=start and (a, w, m) == (HI, HI, 0),
                                stop=(a, w, m) == (LO, HI, M - 1), skip_group_check=True)
                return last

            def product(i, n, j):
                if not has(i, n):
                    return
                if j == 0:
                    pe.wait_ge(xT_ready, block_of(i, n) + 1)
                if not isinstance(i, int) or i > 0 or TB * n + j >= 2:
                    pe.wait_ge(xw_ready, TB * block_of(i, n) + j - 1)
                for a, w in PRODUCTS:
                    for k in range(K):
                        last = nc.tensor.matmul(
                            xp[j % 2][:, :], xT[:, n % 2, a, k, :], wx_part[:, w, k, j, :],
                            start=(a, w, k) == (HI, HI, 0), stop=(a, w, k) == (LO, HI, K - 1))
                last.then_inc(xp_done, 1)

            def keep_warm():
                pe.wait_ge(xw_ready, T)
                for k in range(WARM):
                    nc.tensor.matmul(xp[0][:, :], xT[:, 0, HI, k % K, :], wx_part[:, HI, k % K, 0, :],
                                     start=True, stop=True)

            def turn(i, n, a, half):
                if not has(i, n):
                    return
                if half == 0:
                    pe.wait_ge((x_hi_ready, x_part_ready)[a], block_of(i, n) + 1)
                    if a == HI and has(i, n - 1):
                        pe.wait_ge(xT_ready, block_of(i, n))
                for k in range(half * K // 2, (half + 1) * K // 2):
                    last = nc.tensor.transpose(trp[:, a, k, :], x_part[:, n % 2, a, P * k:P * k + P],
                                               ident[:, :])
                if (a, half) == (LO, 1):
                    last.then_inc(x_turned, 1)

            def step(i, s):
                if not isinstance(i, int) or RING * i + s < T - 1:
                    pe.wait_ge(seeded, RING * i + s + 1)
                product(i, *divmod(s + AHEAD_PRODUCT, J))
                if isinstance(i, int) and T - AHEAD_PRODUCT <= RING * i + s < T - 1:
                    keep_warm()
                n, r = s // TB, s % TB
                if r < 2:
                    turn(i, n + AHEAD_TURN, LO, r)
                else:
                    turn(i, n + AHEAD_TURN + 1, HI, r - 2)
                if isinstance(i, int) and RING * i + s == T - 1:
                    return
                nxt = RING * i + s + 1
                pe.wait_ge(hT_hi_ready, nxt + 1)
                recurrent(gates[(s + 1) % BANKS], (s + 1) % 2, False,
                          lambda: pe.wait_ge(hT_lo_ready, nxt + 1)).then_inc(gates_done, 1)

            pe.wait_ge(const_ready, 3)
            for n in range(1, BANKS):
                last = nc.tensor.matmul(gates[n][:, :], ident[:, :], zeros[:, :], start=True, stop=True)
            last.then_inc(banks_open, 1)
            for a in (HI, LO):
                for half in range(2):
                    turn(0, 0, a, half)
            for a in (HI, LO):
                for half in range(2):
                    turn(0, 1, a, half)
            for j in range(J):
                pe.wait_ge(wx_ready, j + 1)
                product(0, 0, j)
            for n in range(J, AHEAD_PRODUCT):
                product(0, *divmod(n, J))
            pe.wait_ge(wh_ready, J)
            pe.wait_ge(hT_hi_ready, 1)
            recurrent(gates[0], 0, True, lambda: pe.wait_ge(hT_lo_ready, 1)).then_inc(h0_product, 1)
            for half in range(2):
                turn(0, 2, HI, half)
            with pe.Fori(0, LOOPS) as i:
                for s in range(RING):
                    step(i, s)
            for s in range(T - RING * LOOPS):
                step(LOOPS, s)


_INS = ['x', 'cond_1024', 'L0_cond_Wx', 'L0_cond_Wh', 'L0_cond_b']
_OUTS = [((32, 128, 512), 'float32')]


def kernel(**inputs):
    import numpy as _np
    import concourse.bacc as _bacc
    from concourse import mybir as _mybir
    from concourse.bass_utils import run_bass_kernel_spmd as _run

    nc = _bacc.Bacc("TRN2", target_bir_lowering=False, num_devices=1)
    arrays, args = {}, []
    for name in _INS:
        a = _np.ascontiguousarray(inputs[name])
        arrays[f"in_{name}_dram"] = a
        args.append(nc.dram_tensor(f"in_{name}_dram", a.shape, _mybir.dt.from_np(a.dtype), kind="ExternalInput").ap())
    for i, (shape, dtype) in enumerate(_OUTS):
        dt = _mybir.dt.from_np(_np.dtype(dtype))
        args.append(nc.dram_tensor(f"out_{i}_dram", shape, dt, kind="ExternalOutput").ap())
    lstm_kernel(nc, *args)
    r = _run(nc, [arrays], core_ids=[0])
    got = tuple(r.results[0][f"out_{i}_dram"] for i in range(len(_OUTS)))
    return got[0]
```
